# Optimizing a Trainium2 kernel written in Bass

```python
import numpy as np
import jax
import jax.numpy as jnp

def _softmax(x, axis=-1):
    return jax.nn.softmax(x, axis=axis)

def _gelu(x):
    return jax.nn.gelu(x, approximate=True)

def _silu(x):
    return jax.nn.silu(x)

def _sigmoid(x):
    return jax.nn.sigmoid(x)

def _layernorm(x, axis=-1, eps=1e-05):
    m = jnp.mean(x, axis=axis, keepdims=True)
    v = jnp.var(x, axis=axis, keepdims=True)
    return (x - m) / jnp.sqrt(v + eps)

def _scatter_add(tgt, idx, src, axis=0):
    return tgt.at[idx].add(src)

def _segment_sum(src, seg, n):
    return jax.ops.segment_sum(src, seg, n)
kernel_name = 'mk_cond_resid_d1_seqx_r2_cf21ce'

def setup_inputs(seed: int=0):
    np.random.seed(seed)
    _w = jnp.asarray

    def _rec_inputs():
        import jax
        import jax.numpy as jnp
        _rk = jax.random.key(seed)
        x = -0.0003929 + 0.9999 * jax.random.normal(jax.random.fold_in(_rk, 1), (32, 512, 512), jnp.float32)
        _lenS = 512 - jax.random.randint(jax.random.fold_in(_rk, 7), (32,), 0, max(1, 512 // 4) + 1, jnp.int32)
        _lenS2 = 512 - jax.random.randint(jax.random.fold_in(_rk, 8), (32,), 0, max(1, 512 // 4) + 1, jnp.int32)
        fside_Bx1x1024x16_0 = 0.00222621 + 0.99962 * jax.random.normal(jax.random.fold_in(_rk, 11), (32, 1, 512, 16), jnp.float32)
        cond_1024 = -0.00745576 + 0.997402 * jax.random.normal(jax.random.fold_in(_rk, 12), (32, 512), jnp.float32)
        return (x, fside_Bx1x1024x16_0, cond_1024)
    x, fside_Bx1x1024x16_0, cond_1024 = _rec_inputs()

    def _L0_cond_setup():
        import jax, jax.numpy as jnp
        import numpy as np
        B, F_, IN, OUT, R = (32, 256, 512, 512, 16)
        key = jax.random.key(seed)
        ks = jax.random.split(key, 6)
        x = jax.random.normal(ks[0], (B, F_, IN), dtype=jnp.float32)
        u = jax.random.normal(ks[1], (B, 1, OUT, R), dtype=jnp.float32)
        v = jax.random.normal(ks[2], (B, 1, IN, R), dtype=jnp.float32)
        b = jax.random.normal(ks[3], (B, 1, OUT), dtype=jnp.float32)
        lim = 1.0 / np.sqrt(IN)
        W = jax.random.uniform(ks[4], (OUT, IN), minval=-lim, maxval=lim, dtype=jnp.float32)
        fc_bias = jax.random.uniform(ks[5], (OUT,), minval=-lim, maxval=lim, dtype=jnp.float32)
        return {'x': x, 'u': u, 'v': v, 'b': b, 'W': W, 'fc_bias': fc_bias}
    _L0_cond_all = _L0_cond_setup()
    _L0_cond_in = {k: v for k, v in _L0_cond_all.items() if k in ('W', 'fc_bias')}
    del _L0_cond_all
    return {'x': x, 'fside_Bx1x1024x16_0': fside_Bx1x1024x16_0, 'cond_1024': cond_1024, 'L0_cond_W': _L0_cond_in['W'], 'L0_cond_fc_bias': _L0_cond_in['fc_bias']}

def reference(x, fside_Bx1x1024x16_0, cond_1024, L0_cond_W, L0_cond_fc_bias):
    import jax
    import jax.numpy as jnp

    def _L0_cond_ref(x, u, v, b, W, fc_bias):
        import jax, jax.numpy as jnp
        import numpy as np
        B, F_, IN, OUT, R = (32, 256, 512, 512, 16)
        inch = x.shape[-1]
        r = v.shape[-1]
        z1 = jnp.einsum('bfi,bir->bfr', x, v[:, 0]) / inch
        z = jnp.einsum('bfr,bor->bfo', z1, u[:, 0]) / r
        y = jnp.einsum('bfi,oi->bfo', x, W) + fc_bias + z + b
        return jax.nn.gelu(y, approximate=False)
    x = x + _L0_cond_ref(x, fside_Bx1x1024x16_0, fside_Bx1x1024x16_0, cond_1024[:, None, :], L0_cond_W, L0_cond_fc_bias)
    return x

_drawn_inputs = setup_inputs


def setup_inputs(seed=0):
    import zlib

    import numpy as np

    out = dict(_drawn_inputs(seed))
    spreads = {}
    factors = {'fside_Bx1x1024x16_0': 8.0, 'L0_cond_fc_bias': 3.98}
    for name, (base, spread) in spreads.items():
        noise = np.random.default_rng([zlib.crc32(name.encode()), seed]).standard_normal(out[name].shape)
        drawn = base * np.exp(spread * noise) if base else spread * noise
        out[name] = jnp.asarray(drawn.astype(out[name].dtype))
    for name, factor in factors.items():
        out[name] = (out[name] * factor).astype(out[name].dtype)
    return out
```

```python
from contextlib import ExitStack

import concourse.bass as bass
from concourse import mybir

P = 128


def cond_residual_kernel(nc, x_t, w_t, factors, cond, fc_bias, out_t):
    fp32 = mybir.dt.float32
    fp32r = mybir.dt.float32r
    ALU = mybir.AluOpType
    ACT = mybir.ActivationFunctionType

    BATCHES, FEATURES, ROWS = x_t.shape
    CHUNKS = FEATURES // P
    RANK = factors.shape[0] // 4
    UPDATE_SCALE = 1.0 / (FEATURES * RANK)
    X_SLOTS = 4
    SPLIT_SLOTS = 2
    UNROLL = 4
    UPDATE_K = 4 * RANK
    PIECES = 8

    ctx = ExitStack()
    with ctx:
        def sb(name, shape, dt):
            return ctx.enter_context(nc.sbuf_tensor(name, shape, dt))

        def ps(name, shape, dt):
            return ctx.enter_context(nc.psum_tensor(name, shape, dt))

        def sem(name):
            return ctx.enter_context(nc.semaphore(name))

        base_w = sb("base_w", [P, CHUNKS, FEATURES], fp32)
        full_w = sb("full_w", [P, CHUNKS, FEATURES], fp32)
        w_high = [sb(f"w_high{s}", [P, CHUNKS, FEATURES], fp32r) for s in range(SPLIT_SLOTS)]
        w_low = [sb(f"w_low{s}", [P, CHUNKS, FEATURES], fp32r) for s in range(SPLIT_SLOTS)]
        x_in = [sb(f"x_in{s}", [P, CHUNKS, ROWS], fp32) for s in range(X_SLOTS)]
        x_high = [sb(f"x_high{s}", [P, CHUNKS, ROWS], fp32r) for s in range(SPLIT_SLOTS)]
        x_low = [sb(f"x_low{s}", [P, CHUNKS, ROWS], fp32r) for s in range(SPLIT_SLOTS)]
        result = [sb(f"result{s}", [P, CHUNKS, ROWS], fp32) for s in range(SPLIT_SLOTS)]
        f_in = sb("f_in", [4 * RANK, BATCHES // 4, FEATURES], fp32)
        f_high = sb("f_high", [4 * RANK, BATCHES // 4, FEATURES], fp32r)
        f_low = sb("f_low", [4 * RANK, BATCHES // 4, FEATURES], fp32r)
        f_stat = [sb(f"f_stat{s}", [UPDATE_K, FEATURES], fp32r) for s in range(SPLIT_SLOTS)]
        f_mov = [sb(f"f_mov{s}", [UPDATE_K, FEATURES], fp32r) for s in range(SPLIT_SLOTS)]
        cond_sb = sb("cond_sb", [P, BATCHES, CHUNKS], fp32)
        fc_sb = sb("fc_sb", [P, CHUNKS], fp32)
        bias = sb("bias", [P, BATCHES * CHUNKS], fp32)

        update = ps("update", [P, CHUNKS, FEATURES], fp32)
        y = [ps(f"y{m}", [P, ROWS], fp32) for m in range(CHUNKS)]

        w_loaded = sem("w_loaded")
        f_loaded = sem("f_loaded")
        bias_loaded = sem("bias_loaded")
        x_loaded = [sem(f"x_loaded{s}") for s in range(X_SLOTS)]
        f_high_ready = sem("f_high_ready")
        f_low_ready = sem("f_low_ready")
        stacked = [sem(f"stacked{s}") for s in range(SPLIT_SLOTS)]
        bias_ready = sem("bias_ready")
        update_ready = sem("update_ready")
        full_w_ready = sem("full_w_ready")
        w_high_ready = sem("w_high_ready")
        w_low_ready = sem("w_low_ready")
        x_high_ready = sem("x_high_ready")
        x_low_ready = sem("x_low_ready")
        y_ready = sem("y_ready")
        gelu_ready = sem("gelu_ready")
        result_ready = sem("result_ready")
        stored = [sem(f"stored{s}") for s in range(SPLIT_SLOTS)]

        GROUPS = BATCHES // UNROLL

        def batches(engine, step):
            with engine.Fori(0, GROUPS - 1) as t:
                for j in range(UNROLL):
                    step(t, j)
            for j in range(UNROLL):
                step(GROUPS - 1, j)

        block = ctx.enter_context(nc.Block())

        @block.sync
        def _(sp):
            def load_x(t, j):
                sp.dma_start(x_in[j][:, :, :],
                             x_t[UNROLL * t + j].rearrange("(p c) f -> p c f", c=CHUNKS)
                             if isinstance(t, int) else
                             x_t[bass.ds(UNROLL * t + j, 1)].rearrange("a (p c) f -> p (a c) f", c=CHUNKS)
                             ).then_inc(x_loaded[j], 16)

            def place_factors(t, j):
                slot = j % SPLIT_SLOTS
                for g in range(4):
                    for dst, src in ((f_stat[slot], (f_high, f_high, f_low, f_low)[g]),
                                     (f_mov[slot], (f_high, f_low, f_high, f_low)[g])):
                        sp.dma_start(dst[g * RANK:(g + 1) * RANK, :].bitcast(fp32),
                                     src[j * RANK:(j + 1) * RANK, bass.ds(t, 1), :].bitcast(fp32)
                                     ).then_inc(stacked[slot], 16)

            sp.dma_start(f_in[:, :, :], factors).then_inc(f_loaded, 16)
            load_x(0, 0)
            sp.dma_start(base_w[:, :, :], w_t).then_inc(w_loaded, 16)
            sp.dma_start(cond_sb[:, :, :], cond).then_inc(bias_loaded, 16)
            sp.dma_start(fc_sb[:, :], fc_bias).then_inc(bias_loaded, 16)
            sp.wait_ge(f_high_ready, 1)
            sp.wait_ge(f_low_ready, 1)
            place_factors(0, 0)
            place_factors(0, 1)
            for j in range(1, X_SLOTS):
                load_x(0, j)

            def step(t, j):
                b = UNROLL * t + j
                last_group = isinstance(t, int)
                if not (last_group and j >= UNROLL - 2):
                    sp.wait_ge(update_ready, b + 1)
                    place_factors(t + (j + 2) // UNROLL, (j + 2) % UNROLL)
                for half in range(2):
                    sp.wait_ge(result_ready, CHUNKS * b + 2 * (half + 1))
                    src = result[j % SPLIT_SLOTS][:, 2 * half:2 * half + 2, :]
                    dst = out_t[bass.ds(b, 1)] if not last_group else out_t[b:b + 1]
                    dst = dst.rearrange("a (p c) f -> p (a c) f", c=CHUNKS)[:, 2 * half:2 * half + 2, :]
                    sp.dma_start(dst, src).then_inc(stored[j % SPLIT_SLOTS], 16)
                if not last_group:
                    load_x(t + 1, j)

            batches(sp, step)
            for s in range(SPLIT_SLOTS):
                sp.wait_ge(stored[s], 32 * BATCHES // SPLIT_SLOTS)

        @block.scalar
        def _(act):
            def split_x(t, j, started):
                b = UNROLL * t + j
                act.wait_ge(x_loaded[j], 16 * (t + 1))
                if started:
                    act.wait_ge(y_ready, CHUNKS * (b - 1))
                nc.scalar.activation(x_high[j % SPLIT_SLOTS][:, :, :], x_in[j][:, :, :],
                                     ACT.Copy).then_inc(x_high_ready, 1)

            def split_w(t, j):
                b = UNROLL * t + j
                act.wait_ge(full_w_ready, b + 1)
                nc.scalar.activation(w_high[j % SPLIT_SLOTS][:, :, :], full_w[:, :, :],
                                     ACT.Copy).then_inc(w_high_ready, 1)

            act.wait_ge(f_loaded, 16)
            nc.scalar.activation(f_high[:, :, :], f_in[:, :, :], ACT.Copy).then_inc(f_high_ready, 1)
            split_x(0, 0, False)
            split_w(0, 0)
            act.wait_ge(bias_ready, 1)

            def step(t, j, first=False):
                b = UNROLL * t + j
                last = isinstance(t, int) and t == GROUPS - 1 and j == UNROLL - 1
                tn, jn = t + (j + 1) // UNROLL, (j + 1) % UNROLL
                if not last:
                    split_x(tn, jn, not first)
                for m in range(CHUNKS):
                    act.wait_ge(y_ready, CHUNKS * b + m + 1)
                    if m == 0 and not (isinstance(t, int) and b < SPLIT_SLOTS):
                        act.wait_ge(stored[j % SPLIT_SLOTS], 32 * ((b - j % SPLIT_SLOTS) // SPLIT_SLOTS)
                                    if isinstance(t, int) else
                                    32 * (UNROLL // SPLIT_SLOTS) * t + 32 * (j // SPLIT_SLOTS))
                    col = (bias[:, b * CHUNKS + m:b * CHUNKS + m + 1] if isinstance(t, int)
                           else bias[:, bass.ds(b * CHUNKS + m, 1)])
                    nc.scalar.activation(result[j % SPLIT_SLOTS][:, m, :], y[m][:, :], ACT.Gelu,
                                         bias=col).then_inc(gelu_ready, 1)
                    if m == 1 and not last:
                        split_w(tn, jn)

            for j in range(UNROLL):
                step(0, j, first=(j == 0))
            with act.Fori(1, GROUPS - 1) as t:
                for j in range(UNROLL):
                    step(t, j)
            for j in range(UNROLL):
                step(GROUPS - 1, j)

        @block.vector
        def _(dve):
            def low_x(t, j, started):
                b = UNROLL * t + j
                dve.wait_ge(x_high_ready, b + 1)
                nc.vector.tensor_tensor(x_low[j % SPLIT_SLOTS][:, :, :], x_in[j][:, :, :],
                                        x_high[j % SPLIT_SLOTS][:, :, :].bitcast(fp32),
                                        ALU.subtract).then_inc(x_low_ready, 1)

            def full_weights(t, j, started):
                b = UNROLL * t + j
                dve.wait_ge(update_ready, b + 1)
                if started:
                    dve.wait_ge(w_high_ready, b)
                    dve.wait_ge(w_low_ready, b)
                nc.vector.scalar_tensor_tensor(full_w[:, :, :], update[:, :, :], UPDATE_SCALE,
                                               base_w[:, :, :], ALU.mult, ALU.add).then_inc(full_w_ready, 1)

            dve.wait_ge(f_high_ready, 1)
            nc.vector.tensor_tensor(f_low[:, :, :], f_in[:, :, :], f_high[:, :, :].bitcast(fp32),
                                    ALU.subtract).then_inc(f_low_ready, 1)
            low_x(0, 0, False)
            dve.wait_ge(w_loaded, 16)
            full_weights(0, 0, False)
            dve.wait_ge(bias_loaded, 32)
            nc.vector.tensor_tensor(bias[:, :].rearrange("p (b m) -> p b m", m=CHUNKS), cond_sb[:, :, :],
                                    fc_sb[:, :].rearrange("p (a m) -> p a m", a=1).to_broadcast([P, BATCHES, CHUNKS]),
                                    ALU.add).then_inc(bias_ready, 1)

            def step(t, j):
                b = UNROLL * t + j
                last = isinstance(t, int) and t == GROUPS - 1 and j == UNROLL - 1
                tn, jn = t + (j + 1) // UNROLL, (j + 1) % UNROLL
                if not last:
                    low_x(tn, jn, True)
                    full_weights(tn, jn, True)
                for m in range(CHUNKS):
                    dve.wait_ge(gelu_ready, CHUNKS * b + m + 1)
                    nc.vector.tensor_tensor(result[j % SPLIT_SLOTS][:, m, :], result[j % SPLIT_SLOTS][:, m, :],
                                            x_in[j][:, m, :], ALU.add).then_inc(result_ready, 1)

            batches(dve, step)

        @block.gpsimd
        def _(pool):
            def low_w(t, j):
                b = UNROLL * t + j
                pool.wait_ge(w_high_ready, b + 1)
                nc.gpsimd.tensor_tensor(w_low[j % SPLIT_SLOTS][:, :, :], full_w[:, :, :],
                                        w_high[j % SPLIT_SLOTS][:, :, :].bitcast(fp32),
                                        ALU.subtract).then_inc(w_low_ready, 1)

            batches(pool, low_w)

        @block.tensor
        def _(pe):
            def rank_update(t, j, started):
                b = UNROLL * t + j
                slot = j % SPLIT_SLOTS
                pe.wait_ge(stacked[slot], 16 * PIECES * (b // SPLIT_SLOTS + 1) if isinstance(t, int) else
                           16 * PIECES * (UNROLL // SPLIT_SLOTS) * t + 16 * PIECES * (j // SPLIT_SLOTS + 1))
                if started:
                    pe.wait_ge(full_w_ready, b)
                for c in range(CHUNKS):
                    mm = nc.tensor.matmul(update[:, c, :], f_stat[slot][:, c * P:(c + 1) * P],
                                          f_mov[slot][:, :], start=True, stop=True)
                mm.then_inc(update_ready, 1)

            rank_update(0, 0, False)

            def step(t, j, first=False):
                b = UNROLL * t + j
                slot = j % SPLIT_SLOTS
                last = isinstance(t, int) and t == GROUPS - 1 and j == UNROLL - 1
                pe.wait_ge(x_low_ready, b + 1)
                pe.wait_ge(w_low_ready, b + 1)
                for m in range(CHUNKS):
                    if not first:
                        pe.wait_ge(gelu_ready, CHUNKS * (b - 1) + m + 1)
                    for c in range(CHUNKS):
                        cols = slice(m * P, (m + 1) * P)
                        nc.tensor.matmul(y[m][:, :], w_high[slot][:, c, cols], x_high[slot][:, c, :],
                                         start=(c == 0), stop=False)
                        nc.tensor.matmul(y[m][:, :], w_high[slot][:, c, cols], x_low[slot][:, c, :],
                                         start=False, stop=False)
                        mm = nc.tensor.matmul(y[m][:, :], w_low[slot][:, c, cols], x_high[slot][:, c, :],
                                              start=False, stop=(c == CHUNKS - 1))
                    mm.then_inc(y_ready, 1)
                    if m == 0 and not last:
                        rank_update(t + (j + 1) // UNROLL, (j + 1) % UNROLL, True)

            for j in range(UNROLL):
                step(0, j, first=(j == 0))
            with pe.Fori(1, GROUPS - 1) as t:
                for j in range(UNROLL):
                    step(t, j)
            for j in range(UNROLL):
                step(GROUPS - 1, j)


def kernel(x, fside_Bx1x1024x16_0, cond_1024, L0_cond_W, L0_cond_fc_bias):
    import numpy as np
    import concourse.bacc as bacc
    from concourse import mybir as _mybir
    from concourse.bass_utils import run_bass_kernel_spmd

    x = np.asarray(x)
    batches, rows, features = x.shape
    chunks = features // P
    rank = fside_Bx1x1024x16_0.shape[-1]

    x_t = np.ascontiguousarray(x.transpose(0, 2, 1))
    w_t = np.ascontiguousarray(np.asarray(L0_cond_W).reshape(P, chunks, P, chunks).transpose(2, 3, 1, 0)
                               .reshape(P, chunks, features))
    factors = np.asarray(fside_Bx1x1024x16_0).reshape(batches // 4, 4, P, chunks, rank)
    factors = np.ascontiguousarray(factors.transpose(1, 4, 0, 3, 2).reshape(4 * rank, batches // 4, features))
    cond = np.ascontiguousarray(np.asarray(cond_1024).reshape(batches, P, chunks).transpose(1, 0, 2))
    fc_bias = np.ascontiguousarray(np.asarray(L0_cond_fc_bias).reshape(P, chunks))

    nc = bacc.Bacc("TRN2", target_bir_lowering=False, num_devices=1)
    arrays = {"x_t": x_t, "w_t": w_t, "factors": factors, "cond": cond, "fc_bias": fc_bias}
    args = [nc.dram_tensor(name, a.shape, _mybir.dt.from_np(a.dtype), kind="ExternalInput").ap()
            for name, a in arrays.items()]
    out_t = nc.dram_tensor("out_t", x_t.shape, _mybir.dt.float32, kind="ExternalOutput").ap()
    cond_residual_kernel(nc, *args, out_t)
    got = run_bass_kernel_spmd(nc, [arrays], core_ids=[0])
    return np.ascontiguousarray(got.results[0]["out_t"].transpose(0, 2, 1))
```

```python
from contextlib import ExitStack

import concourse.bass as bass
from concourse import mybir

P = 128


def cond_residual_kernel(nc, x_t, w_t, factors, cond, fc_bias, out_t):
    fp32 = mybir.dt.float32
    fp32r = mybir.dt.float32r
    ALU = mybir.AluOpType
    ACT = mybir.ActivationFunctionType

    BATCHES, FEATURES, ROWS = x_t.shape
    CHUNKS = FEATURES // P
    UNROLL = 4
    GROUPS = BATCHES // UNROLL
    RANK = factors.shape[0] // UNROLL
    UPDATE_SCALE = 1.0 / (FEATURES * RANK)
    X_SLOTS = UNROLL
    SLOTS = 2
    STACK = 4
    STACK_DMAS = 5
    HALF = CHUNKS // 2

    ctx = ExitStack()
    with ctx:
        def sb(name, shape, dt):
            return ctx.enter_context(nc.sbuf_tensor(name, shape, dt))

        def ps(name, shape, dt):
            return ctx.enter_context(nc.psum_tensor(name, shape, dt))

        def sem(name):
            return ctx.enter_context(nc.semaphore(name))

        base_w = sb("base_w", [P, CHUNKS, FEATURES], fp32)
        full_w = sb("full_w", [P, CHUNKS, FEATURES], fp32)
        w_high = [sb(f"w_high{s}", [P, CHUNKS, FEATURES], fp32r) for s in range(SLOTS)]
        w_low = [sb(f"w_low{s}", [P, CHUNKS, FEATURES], fp32r) for s in range(SLOTS)]
        x_in = [sb(f"x_in{s}", [P, CHUNKS, ROWS], fp32) for s in range(X_SLOTS)]
        x_high = [sb(f"x_high{s}", [P, CHUNKS, ROWS], fp32r) for s in range(SLOTS)]
        x_low = [sb(f"x_low{s}", [P, CHUNKS, ROWS], fp32r) for s in range(SLOTS)]
        result = [sb(f"result{s}", [P, CHUNKS, ROWS], fp32) for s in range(SLOTS)]
        f_first = sb("f_first", [RANK, FEATURES], fp32)
        f_parts = sb("f_parts", [UNROLL * RANK, GROUPS, 3, FEATURES], fp32)
        f_stack = [sb(f"f_stack{s}", [STACK * RANK, 2, FEATURES], fp32r) for s in range(SLOTS)]
        cond_sb = sb("cond_sb", [P, BATCHES, CHUNKS], fp32)
        fc_sb = sb("fc_sb", [P, CHUNKS], fp32)
        bias = sb("bias", [P, BATCHES * CHUNKS], fp32)

        update = ps("update", [P, CHUNKS, FEATURES], fp32)
        y = [ps(f"y{m}", [P, ROWS], fp32) for m in range(CHUNKS)]

        f_first_loaded = sem("f_first_loaded")
        f_loaded = [sem("f_loaded_group0"), sem("f_loaded_rest")]
        bias_loaded = sem("bias_loaded")
        w_loaded = [sem(f"w_loaded{c}") for c in range(CHUNKS)]
        x_first_loaded = [sem(f"x_first_loaded{c}") for c in range(CHUNKS)]
        x_loaded = [sem(f"x_loaded{s}") for s in range(X_SLOTS)]
        f_high_ready = sem("f_high_ready")
        f_low_ready = sem("f_low_ready")
        stacked = [sem(f"stacked{s}") for s in range(SLOTS)]
        bias_ready = sem("bias_ready")
        update_ready = sem("update_ready")
        full_w_ready = sem("full_w_ready")
        w_high_ready = sem("w_high_ready")
        w_low_ready = sem("w_low_ready")
        x_high_ready = sem("x_high_ready")
        x_low_ready = sem("x_low_ready")
        y_ready = sem("y_ready")
        gelu_ready = sem("gelu_ready")
        result_ready = sem("result_ready")
        stored = [sem(f"stored{s}") for s in range(SLOTS)]

        def made(b):
            return CHUNKS + b

        def batch_chunks(dram, b, chunks):
            return dram[bass.ds(b, 1)].rearrange("a (p c) f -> p (a c) f", c=CHUNKS)[:, chunks, :]

        def groups(engine, step):
            for j in range(UNROLL):
                step(0, j)
            with engine.Fori(1, GROUPS - 1) as t:
                for j in range(UNROLL):
                    step(t, j)
            for j in range(UNROLL):
                step(GROUPS - 1, j)

        def is_first(t, j):
            return isinstance(t, int) and t == 0 and j == 0

        def is_last(t, j):
            return isinstance(t, int) and t == GROUPS - 1 and j == UNROLL - 1

        def next_batch(t, j):
            return t + (j + 1) // UNROLL, (j + 1) % UNROLL

        block = ctx.enter_context(nc.Block())

        @block.sync
        def _(sp):
            def load_x(t, j):
                sp.dma_start(x_in[j][:, :, :],
                             batch_chunks(x_t, UNROLL * t + j, slice(0, CHUNKS))).then_inc(x_loaded[j], 16)

            def stack_factors(t, j):
                parts = f_parts[j * RANK:(j + 1) * RANK, bass.ds(t, 1), :, :].rearrange("r a h i -> r (a h) i")
                slot = j % SLOTS
                high, low = parts[:, 0:1, :], parts[:, 1:2, :]
                for g, sides, pair in ((0, slice(0, 2), high.to_broadcast([RANK, 2, FEATURES])),
                                       (1, slice(0, 2), parts[:, 0:2, :]),
                                       (2, slice(0, 1), low), (2, slice(1, 2), high),
                                       (3, slice(0, 2), low.to_broadcast([RANK, 2, FEATURES]))):
                    sp.dma_start(f_stack[slot][g * RANK:(g + 1) * RANK, sides, :].bitcast(fp32),
                                 pair).then_inc(stacked[slot], 16)

            sp.dma_start(f_first[:, :], factors[0:RANK, 0, :]).then_inc(f_first_loaded, 16)
            for c in range(CHUNKS):
                sp.dma_start(base_w[:, c, :], w_t[:, c, :]).then_inc(w_loaded[c], 16)
                sp.dma_start(x_in[0][:, c, :],
                             x_t[0].rearrange("(p c) f -> p c f", c=CHUNKS)[:, c, :]).then_inc(x_first_loaded[c], 16)
                if c == 1:
                    sp.dma_start(f_parts[:, 0, 2, :], factors[:, 0, :]).then_inc(f_loaded[0], 16)
            sp.dma_start(cond_sb[:, :, :], cond).then_inc(bias_loaded, 16)
            sp.dma_start(fc_sb[:, :], fc_bias).then_inc(bias_loaded, 16)
            load_x(0, 1)
            sp.wait_ge(f_low_ready, 1)
            stack_factors(0, 1)
            stack_factors(0, 2)
            sp.dma_start(f_parts[:, 1:GROUPS, 2, :], factors[:, 1:GROUPS, :]).then_inc(f_loaded[1], 16)
            for j in range(2, X_SLOTS):
                load_x(0, j)

            def step(t, j):
                b = UNROLL * t + j
                last_group = isinstance(t, int) and t == GROUPS - 1
                if not (last_group and j >= UNROLL - 3):
                    t3, j3 = t + (j + 3) // UNROLL, (j + 3) % UNROLL
                    sp.wait_ge(update_ready, made(b + 1))
                    stack_factors(t3, j3)
                for h in range(2):
                    sp.wait_ge(result_ready, 2 * b + h + 1)
                    half = slice(h * HALF, (h + 1) * HALF)
                    sp.dma_start(batch_chunks(out_t, b, half),
                                 result[j % SLOTS][:, half, :]).then_inc(stored[j % SLOTS], 16)
                if j == 0 and not last_group:
                    sp.wait_ge(f_low_ready, t + 2)
                if not last_group:
                    load_x(t + 1, j)

            groups(sp, step)
            for s in range(SLOTS):
                sp.wait_ge(stored[s], 2 * 16 * BATCHES // SLOTS)

        @block.scalar
        def _(act):
            def split_factors(t):
                act.wait_ge(f_loaded[0 if isinstance(t, int) and t == 0 else 1], 16)
                nc.scalar.activation(f_parts[:, bass.ds(t, 1), 0, :].bitcast(fp32r),
                                     f_parts[:, bass.ds(t, 1), 2, :], ACT.Copy).then_inc(f_high_ready, 1)

            def split_x(t, j):
                act.wait_ge(x_loaded[j], 16 * (t + 1) if j else 16 * t)
                b = UNROLL * t + j
                if not (isinstance(t, int) and b < SLOTS):
                    act.wait_ge(y_ready, CHUNKS * (b - 1))
                nc.scalar.activation(x_high[j % SLOTS][:, :, :], x_in[j][:, :, :],
                                     ACT.Copy).then_inc(x_high_ready, 1)

            def split_w(t, j):
                act.wait_ge(full_w_ready, made(UNROLL * t + j))
                nc.scalar.activation(w_high[j % SLOTS][:, :, :], full_w[:, :, :],
                                     ACT.Copy).then_inc(w_high_ready, 1)

            for c in range(CHUNKS):
                act.wait_ge(x_first_loaded[c], 16)
                nc.scalar.activation(x_high[0][:, c, :], x_in[0][:, c, :], ACT.Copy).then_inc(x_high_ready, 1)
                act.wait_ge(full_w_ready, c + 1)
                nc.scalar.activation(w_high[0][:, c, :], full_w[:, c, :], ACT.Copy).then_inc(w_high_ready, 1)
                if c == 1:
                    split_factors(0)
            act.wait_ge(bias_ready, 1)

            def step(t, j):
                b = UNROLL * t + j
                last_group = isinstance(t, int) and t == GROUPS - 1
                tn, jn = next_batch(t, j)
                if not is_last(t, j):
                    split_x(tn, jn)
                if j == 0 and not last_group:
                    split_factors(t + 1)
                for m in range(CHUNKS):
                    act.wait_ge(y_ready, CHUNKS * b + m + 1)
                    if m == 0 and not (isinstance(t, int) and b < SLOTS):
                        act.wait_ge(stored[j % SLOTS], 2 * 16 * (UNROLL // SLOTS * t + j // SLOTS))
                    nc.scalar.activation(result[j % SLOTS][:, m, :], y[m][:, :], ACT.Gelu,
                                         bias=bias[:, bass.ds(b * CHUNKS + m, 1)]).then_inc(gelu_ready, 1)
                    if m == 0 and not is_last(t, j):
                        split_w(tn, jn)
            groups(act, step)

        @block.vector
        def _(dve):
            def low_part(out, whole, high, ready):
                nc.vector.tensor_tensor(out, whole, high.bitcast(fp32), ALU.subtract).then_inc(ready, 1)

            def full_weights(chunks):
                nc.vector.scalar_tensor_tensor(full_w[:, chunks, :], update[:, chunks, :], UPDATE_SCALE,
                                               base_w[:, chunks, :], ALU.mult, ALU.add).then_inc(full_w_ready, 1)

            def low_factors(t):
                dve.wait_ge(f_high_ready, t + 1)
                low_part(f_parts[:, bass.ds(t, 1), 1, :].bitcast(fp32r), f_parts[:, bass.ds(t, 1), 2, :],
                         f_parts[:, bass.ds(t, 1), 0, :], f_low_ready)

            for c in range(CHUNKS):
                one = slice(c, c + 1)
                dve.wait_ge(update_ready, c + 1)
                dve.wait_ge(w_loaded[c], 16)
                full_weights(one)
                dve.wait_ge(x_high_ready, c + 1)
                low_part(x_low[0][:, one, :], x_in[0][:, one, :], x_high[0][:, one, :], x_low_ready)
                dve.wait_ge(w_high_ready, c + 1)
                low_part(w_low[0][:, one, :], full_w[:, one, :], w_high[0][:, one, :], w_low_ready)
                if c == 1:
                    low_factors(0)
            dve.wait_ge(bias_loaded, 2 * 16)
            nc.vector.tensor_tensor(bias[:, :].rearrange("p (b m) -> p b m", m=CHUNKS), cond_sb[:, :, :],
                                    fc_sb[:, :].rearrange("p (a m) -> p a m", a=1)
                                    .to_broadcast([P, BATCHES, CHUNKS]), ALU.add).then_inc(bias_ready, 1)

            def add_x(t, j, h):
                dve.wait_ge(gelu_ready, CHUNKS * (UNROLL * t + j) + (h + 1) * HALF)
                part = result[j % SLOTS][:, h * HALF:(h + 1) * HALF, :]
                nc.vector.tensor_tensor(part, part, x_in[j][:, h * HALF:(h + 1) * HALF, :],
                                        ALU.add).then_inc(result_ready, 1)

            def step(t, j):
                b = UNROLL * t + j
                tn, jn = next_batch(t, j)
                slot = jn % SLOTS
                if not is_last(t, j):
                    dve.wait_ge(update_ready, made(b + 1))
                    dve.wait_ge(w_high_ready, made(b))
                    dve.wait_ge(w_low_ready, made(b))
                    full_weights(slice(0, CHUNKS))
                if not is_first(t, j):
                    tp, jp = (t, j - 1) if j else (t - 1, UNROLL - 1)
                    add_x(tp, jp, 1)
                if not is_last(t, j):
                    dve.wait_ge(x_high_ready, made(b + 1))
                    low_part(x_low[slot][:, :, :], x_in[jn][:, :, :], x_high[slot][:, :, :], x_low_ready)
                    dve.wait_ge(w_high_ready, made(b + 1))
                    low_part(w_low[slot][:, :, :], full_w[:, :, :], w_high[slot][:, :, :], w_low_ready)
                if j == 0 and not (isinstance(t, int) and t == GROUPS - 1):
                    low_factors(t + 1)
                add_x(t, j, 0)

            groups(dve, step)
            add_x(GROUPS - 1, UNROLL - 1, 1)

        @block.tensor
        def _(pe):
            def products(slot, m, c):
                cols = slice(m * P, (m + 1) * P)
                nc.tensor.matmul(y[m][:, :], w_high[slot][:, c, cols], x_high[slot][:, c, :],
                                 start=(c == 0), stop=False)
                nc.tensor.matmul(y[m][:, :], w_high[slot][:, c, cols], x_low[slot][:, c, :],
                                 start=False, stop=False)
                mm = nc.tensor.matmul(y[m][:, :], w_low[slot][:, c, cols], x_high[slot][:, c, :],
                                      start=False, stop=(c == CHUNKS - 1))
                if c == CHUNKS - 1:
                    mm.then_inc(y_ready, 1)

            def first_update(c):
                nc.tensor.matmul(update[:, c, :], f_first[:, c * P:(c + 1) * P], f_first[:, :],
                                 start=True, stop=True).then_inc(update_ready, 1)

            def rank_update(t, j):
                slot = j % SLOTS
                b = UNROLL * t + j
                uses = UNROLL // SLOTS * t + (j // SLOTS + 1 if slot else j // SLOTS)
                pe.wait_ge(stacked[slot], 16 * STACK_DMAS * uses)
                pe.wait_ge(full_w_ready, made(b - 1))
                for c in range(CHUNKS):
                    mm = nc.tensor.matmul(update[:, c, :], f_stack[slot][:, 0, c * P:(c + 1) * P],
                                          f_stack[slot][:, 1, :], start=True, stop=True)
                mm.then_inc(update_ready, 1)

            pe.wait_ge(f_first_loaded, 16)
            first_update(0)
            first_update(1)
            for c in range(CHUNKS):
                if c == 2:
                    rank_update(0, 1)
                pe.wait_ge(x_low_ready, c + 1)
                pe.wait_ge(w_low_ready, c + 1)
                for m in range(CHUNKS):
                    products(0, m, c)
                if c < 2:
                    first_update(c + 2)

            def step(t, j):
                b = UNROLL * t + j
                slot = j % SLOTS
                if is_first(t, j):
                    return
                if not is_last(t, j):
                    rank_update(*next_batch(t, j))
                pe.wait_ge(x_low_ready, made(b))
                pe.wait_ge(w_low_ready, made(b))
                for m in range(CHUNKS):
                    pe.wait_ge(gelu_ready, CHUNKS * (b - 1) + m + 1)
                    for c in range(CHUNKS):
                        products(slot, m, c)

            groups(pe, step)


def kernel(x, fside_Bx1x1024x16_0, cond_1024, L0_cond_W, L0_cond_fc_bias):
    import numpy as np
    import concourse.bacc as bacc
    from concourse import mybir as _mybir
    from concourse.bass_utils import run_bass_kernel_spmd

    x = np.asarray(x)
    batches, rows, features = x.shape
    chunks = features // P
    rank = fside_Bx1x1024x16_0.shape[-1]

    x_t = np.ascontiguousarray(x.transpose(0, 2, 1))
    w_t = np.ascontiguousarray(np.asarray(L0_cond_W).reshape(P, chunks, P, chunks).transpose(2, 3, 1, 0)
                               .reshape(P, chunks, features))
    factors = np.asarray(fside_Bx1x1024x16_0).reshape(batches // 4, 4, P, chunks, rank)
    factors = np.ascontiguousarray(factors.transpose(1, 4, 0, 3, 2).reshape(4 * rank, batches // 4, features))
    cond = np.ascontiguousarray(np.asarray(cond_1024).reshape(batches, P, chunks).transpose(1, 0, 2))
    fc_bias = np.ascontiguousarray(np.asarray(L0_cond_fc_bias).reshape(P, chunks))

    nc = bacc.Bacc("TRN2", target_bir_lowering=False, num_devices=1)
    arrays = {"x_t": x_t, "w_t": w_t, "factors": factors, "cond": cond, "fc_bias": fc_bias}
    args = [nc.dram_tensor(name, a.shape, _mybir.dt.from_np(a.dtype), kind="ExternalInput").ap()
            for name, a in arrays.items()]
    out_t = nc.dram_tensor("out_t", x_t.shape, _mybir.dt.float32, kind="ExternalOutput").ap()
    cond_residual_kernel(nc, *args, out_t)
    got = run_bass_kernel_spmd(nc, [arrays], core_ids=[0])
    return np.ascontiguousarray(got.results[0]["out_t"].transpose(0, 2, 1))
```

```python
from contextlib import ExitStack

import concourse.bass as bass
from concourse import mybir

P = 128
UNROLL = 4


def cond_residual_kernel(nc, x_t, w_t, factors, cond, fc_bias, out_t):
    fp32 = mybir.dt.float32
    fp32r = mybir.dt.float32r
    ALU = mybir.AluOpType
    ACT = mybir.ActivationFunctionType

    BATCHES, FEATURES, ROWS = x_t.shape
    CHUNKS = FEATURES // P
    GROUPS = BATCHES // UNROLL
    RANK = factors.shape[0] // UNROLL
    UPDATE_SCALE = 1.0 / (FEATURES * RANK)
    X_SLOTS = UNROLL
    SLOTS = 2
    STACK = 4
    STACK_DMAS = 5
    HALF = CHUNKS // 2
    PIECEWISE = 2
    WARM_UPS = 5

    ctx = ExitStack()
    with ctx:
        def sb(name, shape, dt):
            return ctx.enter_context(nc.sbuf_tensor(name, shape, dt))

        def ps(name, shape, dt):
            return ctx.enter_context(nc.psum_tensor(name, shape, dt))

        def sem(name):
            return ctx.enter_context(nc.semaphore(name))

        base_w = sb("base_w", [P, CHUNKS, FEATURES], fp32)
        full_w = sb("full_w", [P, CHUNKS, FEATURES], fp32)
        w_high = [sb(f"w_high{s}", [P, CHUNKS, FEATURES], fp32r) for s in range(SLOTS)]
        w_low = [sb(f"w_low{s}", [P, CHUNKS, FEATURES], fp32r) for s in range(SLOTS)]
        x_in = [sb(f"x_in{s}", [P, CHUNKS, ROWS], fp32) for s in range(X_SLOTS)]
        x_high = [sb(f"x_high{s}", [P, CHUNKS, ROWS], fp32r) for s in range(SLOTS)]
        x_low = [sb(f"x_low{s}", [P, CHUNKS, ROWS], fp32r) for s in range(SLOTS)]
        result = [sb(f"result{s}", [P, CHUNKS, ROWS], fp32) for s in range(SLOTS)]
        f_first = sb("f_first", [P, FEATURES], fp32)
        f_parts = sb("f_parts", [UNROLL * RANK, GROUPS, 3, FEATURES], fp32)
        f_stack = [sb(f"f_stack{s}", [P, 2, FEATURES], fp32r) for s in range(SLOTS)]
        cond_sb = sb("cond_sb", [P, BATCHES, CHUNKS], fp32)
        fc_sb = sb("fc_sb", [P, CHUNKS], fp32)
        bias = sb("bias", [P, BATCHES * CHUNKS], fp32)
        idle = sb("idle", [P, ROWS], mybir.dt.bfloat16)
        idle_gelu = sb("idle_gelu", [P, 1], fp32)

        update = ps("update", [P, CHUNKS, FEATURES], fp32)
        y = [ps(f"y{m}", [P, ROWS], fp32) for m in range(CHUNKS)]

        f_first_loaded = sem("f_first_loaded")
        f_loaded = [sem("f_loaded_group0"), sem("f_loaded_rest")]
        bias_loaded = sem("bias_loaded")
        w_loaded = [sem(f"w_loaded{c}") for c in range(CHUNKS)]
        x_first_loaded = [sem(f"x_first_loaded{c}") for c in range(CHUNKS)]
        x_loaded = [sem(f"x_loaded{s}") for s in range(X_SLOTS)]
        f_high_ready = sem("f_high_ready")
        f_low_ready = sem("f_low_ready")
        stacked = [sem(f"stacked{s}") for s in range(SLOTS)]
        bias_ready = sem("bias_ready")
        idle_zeroed = sem("idle_zeroed")
        f_first_zeroed = sem("f_first_zeroed")
        stack_zeroed = sem("stack_zeroed")
        update_ready = sem("update_ready")
        full_w_ready = sem("full_w_ready")
        w_high_ready = sem("w_high_ready")
        w_low_ready = sem("w_low_ready")
        x_high_ready = sem("x_high_ready")
        x_low_ready = sem("x_low_ready")
        y_ready = sem("y_ready")
        gelu_ready = sem("gelu_ready")
        result_ready = sem("result_ready")
        stored = [sem(f"stored{s}") for s in range(SLOTS)]

        def made(b):
            if isinstance(b, int) and b < PIECEWISE:
                return CHUNKS * (b + 1)
            return CHUNKS * PIECEWISE + b - (PIECEWISE - 1)

        def piecewise(t, j):
            return isinstance(t, int) and UNROLL * t + j < PIECEWISE

        def batch_chunks(dram, b, chunks):
            return dram[bass.ds(b, 1)].rearrange("a (p c) f -> p (a c) f", c=CHUNKS)[:, chunks, :]

        def groups(engine, step):
            for j in range(UNROLL):
                step(0, j)
            with engine.Fori(1, GROUPS - 1) as t:
                for j in range(UNROLL):
                    step(t, j)
            for j in range(UNROLL):
                step(GROUPS - 1, j)

        def is_first(t, j):
            return isinstance(t, int) and t == 0 and j == 0

        def is_last(t, j):
            return isinstance(t, int) and t == GROUPS - 1 and j == UNROLL - 1

        def next_batch(t, j):
            return t + (j + 1) // UNROLL, (j + 1) % UNROLL

        block = ctx.enter_context(nc.Block())

        @block.sync
        def _(sp):
            def load_x(t, j):
                sp.dma_start(x_in[j][:, :, :],
                             batch_chunks(x_t, UNROLL * t + j, slice(0, CHUNKS))).then_inc(x_loaded[j], 16)

            def stack_factors(t, j):
                parts = f_parts[j * RANK:(j + 1) * RANK, bass.ds(t, 1), :, :].rearrange("r a h i -> r (a h) i")
                slot = j % SLOTS
                high, low = parts[:, 0:1, :], parts[:, 1:2, :]
                for g, sides, pair in ((0, slice(0, 2), high.to_broadcast([RANK, 2, FEATURES])),
                                       (1, slice(0, 2), parts[:, 0:2, :]),
                                       (2, slice(0, 1), low), (2, slice(1, 2), high),
                                       (3, slice(0, 2), low.to_broadcast([RANK, 2, FEATURES]))):
                    sp.dma_start(f_stack[slot][g * RANK:(g + 1) * RANK, sides, :].bitcast(fp32),
                                 pair).then_inc(stacked[slot], 16)

            for c in range(CHUNKS):
                sp.dma_start(base_w[:, c, :], w_t[:, c, :]).then_inc(w_loaded[c], 16)
                if c == 0:
                    sp.wait_ge(f_first_zeroed, 1)
                    sp.dma_start(f_first[0:RANK, :], factors[0:RANK, 0, :]).then_inc(f_first_loaded, 16)
                if c == 1:
                    sp.dma_start(f_parts[:, 0, 2, :], factors[:, 0, :]).then_inc(f_loaded[0], 16)
                sp.dma_start(x_in[0][:, c, :],
                             x_t[0].rearrange("(p c) f -> p c f", c=CHUNKS)[:, c, :]).then_inc(x_first_loaded[c], 16)
            load_x(0, 1)
            sp.dma_start(cond_sb[:, :, :], cond).then_inc(bias_loaded, 16)
            sp.dma_start(fc_sb[:, :], fc_bias).then_inc(bias_loaded, 16)
            sp.wait_ge(stack_zeroed, SLOTS)
            sp.wait_ge(f_low_ready, 1)
            stack_factors(0, 1)
            stack_factors(0, 2)
            sp.dma_start(f_parts[:, 1:GROUPS, 2, :], factors[:, 1:GROUPS, :]).then_inc(f_loaded[1], 16)
            for j in range(2, X_SLOTS):
                load_x(0, j)

            def step(t, j):
                b = UNROLL * t + j
                last_group = isinstance(t, int) and t == GROUPS - 1
                if not (last_group and j >= UNROLL - 3):
                    t3, j3 = t + (j + 3) // UNROLL, (j + 3) % UNROLL
                    sp.wait_ge(update_ready, made(b + 1))
                    stack_factors(t3, j3)
                parts = [slice(0, HALF), slice(HALF, CHUNKS)]
                if is_last(t, j):
                    parts[1:] = [slice(m, m + 1) for m in range(HALF, CHUNKS)]
                for n, part in enumerate(parts):
                    sp.wait_ge(result_ready, 2 * b + n + 1)
                    sp.dma_start(batch_chunks(out_t, b, part),
                                 result[j % SLOTS][:, part, :]).then_inc(stored[j % SLOTS], 16)
                if j == 0 and not last_group:
                    sp.wait_ge(f_low_ready, t + 2)
                if not last_group:
                    load_x(t + 1, j)

            groups(sp, step)
            sp.wait_ge(stored[0], 2 * 16 * BATCHES // SLOTS)
            sp.wait_ge(stored[1], 2 * 16 * BATCHES // SLOTS + 16 * (HALF - 1))

        @block.scalar
        def _(act):
            def split_factors(t):
                act.wait_ge(f_loaded[0 if isinstance(t, int) and t == 0 else 1], 16)
                nc.scalar.activation(f_parts[:, bass.ds(t, 1), 0, :].bitcast(fp32r),
                                     f_parts[:, bass.ds(t, 1), 2, :], ACT.Copy).then_inc(f_high_ready, 1)

            def split_x(t, j):
                act.wait_ge(x_loaded[j], 16 * (t + 1) if j else 16 * t)
                b = UNROLL * t + j
                if not (isinstance(t, int) and b < SLOTS):
                    act.wait_ge(y_ready, CHUNKS * (b - 1))
                nc.scalar.activation(x_high[j % SLOTS][:, :, :], x_in[j][:, :, :],
                                     ACT.Copy).then_inc(x_high_ready, 1)

            def split_w(t, j):
                act.wait_ge(full_w_ready, made(UNROLL * t + j))
                nc.scalar.activation(w_high[j % SLOTS][:, :, :], full_w[:, :, :],
                                     ACT.Copy).then_inc(w_high_ready, 1)

            def high_pieces(b, c):
                if b == 0:
                    act.wait_ge(x_first_loaded[c], 16)
                else:
                    act.wait_ge(x_loaded[b], 16)
                nc.scalar.activation(x_high[b][:, c, :], x_in[b][:, c, :], ACT.Copy).then_inc(x_high_ready, 1)
                act.wait_ge(full_w_ready, CHUNKS * b + c + 1)
                nc.scalar.activation(w_high[b][:, c, :], full_w[:, c, :], ACT.Copy).then_inc(w_high_ready, 1)

            act.wait_ge(idle_zeroed, 1)
            nc.scalar.activation(idle_gelu[:, :], idle[:, 0:1], ACT.Gelu)
            for c in range(CHUNKS):
                high_pieces(0, c)
                if c == 0:
                    split_factors(0)

            def step(t, j):
                b = UNROLL * t + j
                last_group = isinstance(t, int) and t == GROUPS - 1
                tn, jn = next_batch(t, j)
                if piecewise(tn, jn):
                    for c in range(CHUNKS // 2):
                        high_pieces(b + 1, c)
                elif not is_last(t, j):
                    split_x(tn, jn)
                    if piecewise(t, j):
                        split_w(tn, jn)
                for m in range(CHUNKS):
                    act.wait_ge(y_ready, CHUNKS * b + m + 1)
                    if m == 0 and not (isinstance(t, int) and b < SLOTS):
                        act.wait_ge(stored[j % SLOTS], 2 * 16 * (UNROLL // SLOTS * t + j // SLOTS))
                    if m == 0 and is_first(t, j):
                        act.wait_ge(bias_ready, 1)
                    nc.scalar.activation(result[j % SLOTS][:, m, :], y[m][:, :], ACT.Gelu,
                                         bias=bias[:, bass.ds(b * CHUNKS + m, 1)]).then_inc(gelu_ready, 1)
                    if m == 0 and not is_last(t, j) and not piecewise(t, j):
                        split_w(tn, jn)
                if piecewise(tn, jn):
                    for c in range(CHUNKS // 2, CHUNKS):
                        high_pieces(b + 1, c)
                if j == 0 and not last_group:
                    split_factors(t + 1)

            groups(act, step)

        @block.vector
        def _(dve):
            def low_part(out, whole, high, ready):
                nc.vector.tensor_tensor(out, whole, high.bitcast(fp32), ALU.subtract).then_inc(ready, 1)

            def full_weights(chunks):
                nc.vector.scalar_tensor_tensor(full_w[:, chunks, :], update[:, chunks, :], UPDATE_SCALE,
                                               base_w[:, chunks, :], ALU.mult, ALU.add).then_inc(full_w_ready, 1)

            def low_factors(t):
                dve.wait_ge(f_high_ready, t + 1)
                low_part(f_parts[:, bass.ds(t, 1), 1, :].bitcast(fp32r), f_parts[:, bass.ds(t, 1), 2, :],
                         f_parts[:, bass.ds(t, 1), 0, :], f_low_ready)

            def pieces(b, c):
                n, one = CHUNKS * b + c + 1, slice(c, c + 1)
                dve.wait_ge(update_ready, n)
                if b == 0:
                    dve.wait_ge(w_loaded[c], 16)
                else:
                    dve.wait_ge(w_high_ready, n - CHUNKS)
                    dve.wait_ge(w_low_ready, n - CHUNKS)
                full_weights(one)
                dve.wait_ge(x_high_ready, n)
                low_part(x_low[b][:, one, :], x_in[b][:, one, :], x_high[b][:, one, :], x_low_ready)
                dve.wait_ge(w_high_ready, n)
                low_part(w_low[b][:, one, :], full_w[:, one, :], w_high[b][:, one, :], w_low_ready)

            nc.vector.memset(f_first[:, :], 0.0).then_inc(f_first_zeroed, 1)
            for s in range(SLOTS):
                nc.vector.memset(f_stack[s][STACK * RANK:P, :, :].bitcast(fp32), 0.0).then_inc(stack_zeroed, 1)
            for c in range(CHUNKS):
                pieces(0, c)
                if c == 0:
                    low_factors(0)
            dve.wait_ge(bias_loaded, 2 * 16)
            nc.vector.tensor_tensor(bias[:, :].rearrange("p (b m) -> p b m", m=CHUNKS), cond_sb[:, :, :],
                                    fc_sb[:, :].rearrange("p (a m) -> p a m", a=1)
                                    .to_broadcast([P, BATCHES, CHUNKS]), ALU.add).then_inc(bias_ready, 1)

            def add_x(t, j, chunks):
                dve.wait_ge(gelu_ready, CHUNKS * (UNROLL * t + j) + chunks.stop)
                part = result[j % SLOTS][:, chunks, :]
                nc.vector.tensor_tensor(part, part, x_in[j][:, chunks, :], ALU.add).then_inc(result_ready, 1)

            def finish_previous(t, j):
                if not is_first(t, j):
                    tp, jp = (t, j - 1) if j else (t - 1, UNROLL - 1)
                    add_x(tp, jp, slice(HALF, CHUNKS))
                if j == 1 and not (isinstance(t, int) and t == GROUPS - 1):
                    low_factors(t + 1)

            def step(t, j):
                b = UNROLL * t + j
                tn, jn = next_batch(t, j)
                slot = jn % SLOTS
                if piecewise(tn, jn):
                    for c in range(CHUNKS):
                        pieces(b + 1, c)
                elif not is_last(t, j):
                    dve.wait_ge(update_ready, made(b + 1))
                    dve.wait_ge(w_high_ready, made(b))
                    dve.wait_ge(w_low_ready, made(b))
                    full_weights(slice(0, CHUNKS))
                if not piecewise(t, j):
                    finish_previous(t, j)
                if not is_last(t, j) and not piecewise(tn, jn):
                    dve.wait_ge(x_high_ready, made(b + 1))
                    low_part(x_low[slot][:, :, :], x_in[jn][:, :, :], x_high[slot][:, :, :], x_low_ready)
                    dve.wait_ge(w_high_ready, made(b + 1))
                    low_part(w_low[slot][:, :, :], full_w[:, :, :], w_high[slot][:, :, :], w_low_ready)
                if piecewise(t, j):
                    finish_previous(t, j)
                add_x(t, j, slice(0, HALF))

            groups(dve, step)
            for m in range(HALF, CHUNKS):
                add_x(GROUPS - 1, UNROLL - 1, slice(m, m + 1))

        @block.gpsimd
        def _(pool):
            nc.gpsimd.memset(idle[:, :], 0.0).then_inc(idle_zeroed, 1)

        @block.tensor
        def _(pe):
            def high_high(slot, m, c):
                nc.tensor.matmul(y[m][:, :], w_high[slot][:, c, m * P:(m + 1) * P], x_high[slot][:, c, :],
                                 start=(c == 0), stop=False)

            def high_low(slot, m, c):
                nc.tensor.matmul(y[m][:, :], w_high[slot][:, c, m * P:(m + 1) * P], x_low[slot][:, c, :],
                                 start=False, stop=False)

            def low_high(slot, m, c):
                mm = nc.tensor.matmul(y[m][:, :], w_low[slot][:, c, m * P:(m + 1) * P], x_high[slot][:, c, :],
                                      start=False, stop=(c == CHUNKS - 1))
                if c == CHUNKS - 1:
                    mm.then_inc(y_ready, 1)

            def piece(b, c):
                n = CHUNKS * b + c + 1
                if c == CHUNKS - 1:
                    pe.wait_ge(x_low_ready, n)
                    pe.wait_ge(w_low_ready, n)
                    for m in range(CHUNKS):
                        high_high(b, m, c)
                        high_low(b, m, c)
                        low_high(b, m, c)
                    return
                pe.wait_ge(x_high_ready, n)
                pe.wait_ge(w_high_ready, n)
                for m in range(CHUNKS):
                    if b > 0 and c == 0:
                        pe.wait_ge(gelu_ready, CHUNKS * (b - 1) + m + 1)
                    high_high(b, m, c)
                pe.wait_ge(x_low_ready, n)
                for m in range(CHUNKS):
                    high_low(b, m, c)
                pe.wait_ge(w_low_ready, n)
                for m in range(CHUNKS):
                    low_high(b, m, c)

            def first_update(c):
                nc.tensor.matmul(update[:, c, :], f_first[:, c * P:(c + 1) * P], f_first[:, :],
                                 start=True, stop=True).then_inc(update_ready, 1)

            def rank_update(t, j):
                slot = j % SLOTS
                b = UNROLL * t + j
                uses = UNROLL // SLOTS * t + (j // SLOTS + 1 if slot else j // SLOTS)
                pe.wait_ge(stacked[slot], 16 * STACK_DMAS * uses)
                if piecewise(t, j):
                    pe.wait_ge(stack_zeroed, SLOTS)
                pe.wait_ge(full_w_ready, made(b - 1))
                for c in range(CHUNKS):
                    mm = nc.tensor.matmul(update[:, c, :], f_stack[slot][:, 0, c * P:(c + 1) * P],
                                          f_stack[slot][:, 1, :], start=True, stop=True)
                    if piecewise(t, j) or c == CHUNKS - 1:
                        mm.then_inc(update_ready, 1)

            pe.wait_ge(idle_zeroed, 1)
            for _ in range(WARM_UPS):
                nc.tensor.matmul(y[0][:, :], idle[:, 0:P], idle[:, :], start=True, stop=True)
            pe.wait_ge(f_first_loaded, 16)
            for c in range(CHUNKS - 1):
                first_update(c)
            for c in range(CHUNKS):
                if c == 1:
                    first_update(CHUNKS - 1)
                if c == CHUNKS // 2:
                    rank_update(0, 1)
                piece(0, c)

            def step(t, j):
                b = UNROLL * t + j
                slot = j % SLOTS
                if is_first(t, j):
                    return
                if piecewise(t, j):
                    for c in range(CHUNKS):
                        if c == CHUNKS // 2:
                            rank_update(*next_batch(t, j))
                        piece(b, c)
                    return
                if not is_last(t, j):
                    rank_update(*next_batch(t, j))
                pe.wait_ge(w_high_ready, made(b))
                pe.wait_ge(x_low_ready, made(b))
                for m in range(CHUNKS):
                    pe.wait_ge(gelu_ready, CHUNKS * (b - 1) + m + 1)
                    for c in range(CHUNKS):
                        high_high(slot, m, c)
                        high_low(slot, m, c)
                    if m == 0:
                        pe.wait_ge(w_low_ready, made(b))
                    for c in range(CHUNKS):
                        low_high(slot, m, c)

            groups(pe, step)


def kernel(x, fside_Bx1x1024x16_0, cond_1024, L0_cond_W, L0_cond_fc_bias):
    import numpy as np
    import concourse.bacc as bacc
    from concourse import mybir as _mybir
    from concourse.bass_utils import run_bass_kernel_spmd

    x = np.asarray(x)
    batches, rows, features = x.shape
    chunks = features // P
    rank = fside_Bx1x1024x16_0.shape[-1]

    x_t = np.ascontiguousarray(x.transpose(0, 2, 1))
    w_t = np.ascontiguousarray(np.asarray(L0_cond_W).reshape(P, chunks, P, chunks).transpose(2, 3, 1, 0)
                               .reshape(P, chunks, features))
    factors = np.asarray(fside_Bx1x1024x16_0).reshape(batches // UNROLL, UNROLL, P, chunks, rank)
    factors = np.ascontiguousarray(factors.transpose(1, 4, 0, 3, 2).reshape(UNROLL * rank, batches // UNROLL, features))
    cond = np.ascontiguousarray(np.asarray(cond_1024).reshape(batches, P, chunks).transpose(1, 0, 2))
    fc_bias = np.ascontiguousarray(np.asarray(L0_cond_fc_bias).reshape(P, chunks))

    nc = bacc.Bacc("TRN2", target_bir_lowering=False, num_devices=1)
    arrays = {"x_t": x_t, "w_t": w_t, "factors": factors, "cond": cond, "fc_bias": fc_bias}
    args = [nc.dram_tensor(name, a.shape, _mybir.dt.from_np(a.dtype), kind="ExternalInput").ap()
            for name, a in arrays.items()]
    out_t = nc.dram_tensor("out_t", x_t.shape, _mybir.dt.float32, kind="ExternalOutput").ap()
    cond_residual_kernel(nc, *args, out_t)
    got = run_bass_kernel_spmd(nc, [arrays], core_ids=[0])
    return np.ascontiguousarray(got.results[0]["out_t"].transpose(0, 2, 1))
```
